# Optimizing a Trainium2 kernel written in Bass

```python
import numpy as np
import jax
import jax.numpy as jnp

def _softmax(x, axis=-1):
    return jax.nn.softmax(x, axis=axis)

def _gelu(x):
    return jax.nn.gelu(x, approximate=True)

def _silu(x):
    return jax.nn.silu(x)

def _sigmoid(x):
    return jax.nn.sigmoid(x)

def _layernorm(x, axis=-1, eps=1e-05):
    m = jnp.mean(x, axis=axis, keepdims=True)
    v = jnp.var(x, axis=axis, keepdims=True)
    return (x - m) / jnp.sqrt(v + eps)

def _scatter_add(tgt, idx, src, axis=0):
    return tgt.at[idx].add(src)

def _segment_sum(src, seg, n):
    return jax.ops.segment_sum(src, seg, n)
kernel_name = 'mk_prb_d1_jaxref_r8_dec8e2'

def setup_inputs(seed: int=0):
    np.random.seed(seed)
    _w = jnp.asarray

    def _L0_attn_setup():
        import jax, jax.numpy as jnp
        import numpy as np
        D_MODEL = 256
        N_HEADS = 16
        D_K = 128
        EPS = 1e-05
        ROPE_BASE = 10000.0

        def rope(x):
            b, s, h, d = x.shape
            d2 = d // 2
            theta = 1.0 / ROPE_BASE ** (jnp.arange(0, d, 2, dtype=jnp.float32) / d)
            pos = jnp.arange(s, dtype=jnp.float32)
            freqs = pos[:, None] * theta[None, :]
            freqs = jnp.concatenate([freqs, freqs], axis=-1)
            cos = jnp.cos(freqs)[None, :, None, :]
            sin = jnp.sin(freqs)[None, :, None, :]
            x_rot = jnp.concatenate([-x[..., d2:], x[..., :d2]], axis=-1)
            return x * cos + x_rot * sin
        key = jax.random.key(seed)
        ks = jax.random.split(key, 10)
        hd = N_HEADS * D_K

        def xavier(k, shape):
            fan_in, fan_out = (shape[1], shape[0])
            lim = np.sqrt(6.0 / (fan_in + fan_out))
            return jax.random.uniform(k, shape, jnp.float32, -lim, lim)
        return {'h': jax.random.normal(ks[0], (2, 256, D_MODEL), jnp.float32), 'wq': xavier(ks[1], (hd, D_MODEL)), 'bq': jnp.zeros((hd,), jnp.float32), 'wk': xavier(ks[2], (hd, D_MODEL)), 'bk': jnp.zeros((hd,), jnp.float32), 'wv': xavier(ks[3], (hd, D_MODEL)), 'bv': jnp.zeros((hd,), jnp.float32), 'wo': xavier(ks[4], (D_MODEL, hd)), 'bo': jnp.zeros((D_MODEL,), jnp.float32), 'ln_g': jnp.ones((D_MODEL,), jnp.float32), 'ln_b': jnp.zeros((D_MODEL,), jnp.float32)}
    _L0_attn_in = _L0_attn_setup()

    def _L0_ffn_setup():
        import jax, jax.numpy as jnp
        import numpy as np
        E = 32
        K = 4
        G = 4
        TG = 2
        H = 256
        F = 128
        FS = 256
        SCALE = 2.0
        B, S = (2, 128)
        N = B * S
        CAP = 2 * (N * K // E)

        def _gate(x, gate_w, gate_bias):
            logits = x @ gate_w.T
            scores = jax.nn.sigmoid(logits)
            sc = scores + gate_bias
            n = x.shape[0]
            grp = sc.reshape(n, G, E // G)
            group_scores = jax.lax.top_k(grp, 2)[0].sum(-1)
            _, gidx = jax.lax.top_k(group_scores, TG)
            gmask = jnp.zeros((n, G), sc.dtype).at[jnp.arange(n)[:, None], gidx].set(1.0)
            smask = jnp.repeat(gmask, E // G, axis=1)
            tmp = jnp.where(smask > 0, sc, 0.0)
            _, topk_idx = jax.lax.top_k(tmp, K)
            topk_w = jnp.take_along_axis(scores, topk_idx, axis=1)
            topk_w = topk_w / (topk_w.sum(-1, keepdims=True) + 1e-20)
            return (topk_idx, topk_w * SCALE)

        def _moe(x, topk_idx, topk_w, w1, w2, w3):
            n = x.shape[0]
            flat_e = topk_idx.reshape(-1)
            oh = jax.nn.one_hot(flat_e, E, dtype=jnp.int32)
            pos = (jnp.cumsum(oh, axis=0) * oh).sum(-1) - 1
            keep = pos < CAP
            slot = jnp.where(keep, pos, CAP)
            x_rep = jnp.repeat(x, K, axis=0)
            buf = jnp.zeros((E, CAP, H), x.dtype).at[flat_e, slot].set(x_rep, mode='drop')
            h = jax.nn.silu(jnp.einsum('ech,ehf->ecf', buf, w1)) * jnp.einsum('ech,ehf->ecf', buf, w3)
            ob = jnp.einsum('ecf,efh->ech', h, w2)
            y = ob[flat_e, jnp.minimum(slot, CAP - 1)]
            y = jnp.where(keep[:, None], y, 0.0)
            return (y.reshape(n, K, H) * topk_w[:, :, None]).sum(1)
        key = jax.random.key(seed)
        ks = jax.random.split(key, 9)
        w = 0.02
        return {'hidden_states': jax.random.normal(ks[0], (B, S, H), jnp.float32), 'gate_w': jax.random.normal(ks[1], (E, H), jnp.float32) * w, 'gate_bias': jax.random.normal(ks[2], (E,), jnp.float32) * w, 'w1': jax.random.normal(ks[3], (E, H, F), jnp.float32) * w, 'w2': jax.random.normal(ks[4], (E, F, H), jnp.float32) * w, 'w3': jax.random.normal(ks[5], (E, H, F), jnp.float32) * w, 'shared_gate': jax.random.normal(ks[6], (H, FS), jnp.float32) * w, 'shared_up': jax.random.normal(ks[7], (H, FS), jnp.float32) * w, 'shared_down': jax.random.normal(ks[8], (FS, H), jnp.float32) * w}
    _L0_ffn_in = _L0_ffn_setup()
    _d = {'L0_attn_h': _L0_attn_in['h'], 'L0_attn_wq': _L0_attn_in['wq'], 'L0_attn_bq': _L0_attn_in['bq'], 'L0_attn_wk': _L0_attn_in['wk'], 'L0_attn_bk': _L0_attn_in['bk'], 'L0_attn_wv': _L0_attn_in['wv'], 'L0_attn_bv': _L0_attn_in['bv'], 'L0_attn_wo': _L0_attn_in['wo'], 'L0_attn_bo': _L0_attn_in['bo'], 'L0_attn_ln_g': _L0_attn_in['ln_g'], 'L0_attn_ln_b': _L0_attn_in['ln_b'], 'L0_ffn_gate_w': _L0_ffn_in['gate_w'], 'L0_ffn_gate_bias': _L0_ffn_in['gate_bias'], 'L0_ffn_w1': _L0_ffn_in['w1'], 'L0_ffn_w2': _L0_ffn_in['w2'], 'L0_ffn_w3': _L0_ffn_in['w3'], 'L0_ffn_shared_gate': _L0_ffn_in['shared_gate'], 'L0_ffn_shared_up': _L0_ffn_in['shared_up'], 'L0_ffn_shared_down': _L0_ffn_in['shared_down']}
    _x0 = _d['L0_attn_h']
    _d['L0_attn_h'] = jax.random.normal(jax.random.fold_in(jax.random.key(seed), 1), (2, 1024, 256), dtype=_x0.dtype)
    del _x0
    return _d

def reference(L0_attn_h, L0_attn_wq, L0_attn_bq, L0_attn_wk, L0_attn_bk, L0_attn_wv, L0_attn_bv, L0_attn_wo, L0_attn_bo, L0_attn_ln_g, L0_attn_ln_b, L0_ffn_gate_w, L0_ffn_gate_bias, L0_ffn_w1, L0_ffn_w2, L0_ffn_w3, L0_ffn_shared_gate, L0_ffn_shared_up, L0_ffn_shared_down):

    def _L0_attn_ref(h, wq, bq, wk, bk, wv, bv, wo, bo, ln_g, ln_b):
        import jax, jax.numpy as jnp
        import numpy as np
        D_MODEL = 256
        N_HEADS = 16
        D_K = 128
        EPS = 1e-05
        ROPE_BASE = 10000.0

        def rope(x):
            b, s, h, d = x.shape
            d2 = d // 2
            theta = 1.0 / ROPE_BASE ** (jnp.arange(0, d, 2, dtype=jnp.float32) / d)
            pos = jnp.arange(s, dtype=jnp.float32)
            freqs = pos[:, None] * theta[None, :]
            freqs = jnp.concatenate([freqs, freqs], axis=-1)
            cos = jnp.cos(freqs)[None, :, None, :]
            sin = jnp.sin(freqs)[None, :, None, :]
            x_rot = jnp.concatenate([-x[..., d2:], x[..., :d2]], axis=-1)
            return x * cos + x_rot * sin
        residual = h
        mu = jnp.mean(h, axis=-1, keepdims=True)
        var = jnp.mean(jnp.square(h - mu), axis=-1, keepdims=True)
        x = (h - mu) * jax.lax.rsqrt(var + EPS) * ln_g + ln_b
        b, s, _ = x.shape
        q = (x @ wq.T + bq).reshape(b, s, N_HEADS, D_K)
        k = (x @ wk.T + bk).reshape(b, s, N_HEADS, D_K)
        v = (x @ wv.T + bv).reshape(b, s, N_HEADS, D_K)
        q = rope(q)
        k = rope(k)
        scale = 1.0 / np.sqrt(D_K)
        attn = jnp.einsum('bihd,bjhd->bhij', q, k) * scale
        causal = jnp.triu(jnp.ones((s, s), dtype=bool), k=1)
        attn = jnp.where(causal[None, None], -jnp.inf, attn)
        attn = jax.nn.softmax(attn, axis=-1)
        o = jnp.einsum('bhij,bjhd->bihd', attn, v).reshape(b, s, N_HEADS * D_K)
        return o @ wo.T + bo + residual

    def _L0_ffn_ref(hidden_states, gate_w, gate_bias, w1, w2, w3, shared_gate, shared_up, shared_down):
        import jax, jax.numpy as jnp
        import numpy as np
        E = 32
        K = 4
        G = 4
        TG = 2
        H = 256
        F = 128
        FS = 256
        SCALE = 2.0
        B, S = (2, 128)
        N = B * S
        CAP = 2 * (N * K // E)

        def _gate(x, gate_w, gate_bias):
            logits = x @ gate_w.T
            scores = jax.nn.sigmoid(logits)
            sc = scores + gate_bias
            n = x.shape[0]
            grp = sc.reshape(n, G, E // G)
            group_scores = jax.lax.top_k(grp, 2)[0].sum(-1)
            _, gidx = jax.lax.top_k(group_scores, TG)
            gmask = jnp.zeros((n, G), sc.dtype).at[jnp.arange(n)[:, None], gidx].set(1.0)
            smask = jnp.repeat(gmask, E // G, axis=1)
            tmp = jnp.where(smask > 0, sc, 0.0)
            _, topk_idx = jax.lax.top_k(tmp, K)
            topk_w = jnp.take_along_axis(scores, topk_idx, axis=1)
            topk_w = topk_w / (topk_w.sum(-1, keepdims=True) + 1e-20)
            return (topk_idx, topk_w * SCALE)

        def _moe(x, topk_idx, topk_w, w1, w2, w3):
            n = x.shape[0]
            flat_e = topk_idx.reshape(-1)
            oh = jax.nn.one_hot(flat_e, E, dtype=jnp.int32)
            pos = (jnp.cumsum(oh, axis=0) * oh).sum(-1) - 1
            keep = pos < CAP
            slot = jnp.where(keep, pos, CAP)
            x_rep = jnp.repeat(x, K, axis=0)
            buf = jnp.zeros((E, CAP, H), x.dtype).at[flat_e, slot].set(x_rep, mode='drop')
            h = jax.nn.silu(jnp.einsum('ech,ehf->ecf', buf, w1)) * jnp.einsum('ech,ehf->ecf', buf, w3)
            ob = jnp.einsum('ecf,efh->ech', h, w2)
            y = ob[flat_e, jnp.minimum(slot, CAP - 1)]
            y = jnp.where(keep[:, None], y, 0.0)
            return (y.reshape(n, K, H) * topk_w[:, :, None]).sum(1)
        b, s, h = hidden_states.shape
        x = hidden_states.reshape(-1, h)
        topk_idx, topk_w = _gate(x, gate_w, gate_bias)
        out = _moe(x, topk_idx, topk_w, w1, w2, w3)
        shared = jax.nn.silu(x @ shared_gate) * (x @ shared_up) @ shared_down
        return (out + shared).reshape(b, s, h)
    x = L0_attn_h
    xn = _layernorm(x, axis=-1)
    x = x + _L0_attn_ref(xn, L0_attn_wq, L0_attn_bq, L0_attn_wk, L0_attn_bk, L0_attn_wv, L0_attn_bv, L0_attn_wo, L0_attn_bo, L0_attn_ln_g, L0_attn_ln_b) + _L0_ffn_ref(xn, L0_ffn_gate_w, L0_ffn_gate_bias, L0_ffn_w1, L0_ffn_w2, L0_ffn_w3, L0_ffn_shared_gate, L0_ffn_shared_up, L0_ffn_shared_down)
    return x

_drawn_inputs = setup_inputs


def setup_inputs(seed=0):
    import zlib

    import numpy as np

    out = dict(_drawn_inputs(seed))
    spreads = {'L0_attn_bq': (0.0, 0.8),
     'L0_attn_bk': (0.0, 0.8),
     'L0_attn_bv': (0.0, 0.457),
     'L0_attn_bo': (0.0, 0.671),
     'L0_attn_ln_g': (1.0, 0.6),
     'L0_attn_ln_b': (0.0, 0.276)}
    factors = {'L0_attn_wq': 7.703,
     'L0_attn_wk': 7.377,
     'L0_ffn_gate_w': 8.0,
     'L0_ffn_gate_bias': 8.0,
     'L0_ffn_w1': 8.0,
     'L0_ffn_w2': 8.0,
     'L0_ffn_w3': 8.0,
     'L0_ffn_shared_gate': 6.852,
     'L0_ffn_shared_up': 6.784,
     'L0_ffn_shared_down': 6.757}
    for name, (base, spread) in spreads.items():
        noise = np.random.default_rng([zlib.crc32(name.encode()), seed]).standard_normal(out[name].shape)
        drawn = base * np.exp(spread * noise) if base else spread * noise
        out[name] = jnp.asarray(drawn.astype(out[name].dtype))
    for name, factor in factors.items():
        out[name] = (out[name] * factor).astype(out[name].dtype)
    return out
```

```python
from contextlib import ExitStack

import concourse.bass as bass
from concourse import mybir

F32 = mybir.dt.float32
F32R = mybir.dt.float32r
BF16 = mybir.dt.bfloat16
F16 = mybir.dt.float16
U32 = mybir.dt.uint32
ALU = mybir.AluOpType
ACT = mybir.ActivationFunctionType
AX = mybir.AxisListType

P = 128
BATCH, SEQ, DM = 2, 1024, 256
TOK = BATCH * SEQ
HEADS, DK = 16, 128
KC = DM // P
TILES = SEQ // P
CH = 512
NG = TOK // CH
GT = CH // P
NT = TOK // P
EXPERTS, TOPK, GROUPS, TOPG = 32, 4, 4, 2
EG = EXPERTS // GROUPS
FE = 128
FS = 256
CAP = 64
EPS = 1e-5
SCALE = DK ** -0.5
ROUTE_SCALE = 2.0
NEG = -1e30
UNITS = HEADS * BATCH
WP = 3 * KC * DK
WO = DM
WROW = WP + WO + 3
EROW = 2 * KC * FE + DM
TROW = DM + EXPERTS
assert UNITS == EXPERTS and HEADS * DK == 2048 and CAP * 2 == P

C_ID, C_MASK, C_COS, C_SIN = 0, P, 2 * P, 2 * P + SEQ
C_IOTA = C_SIN + SEQ
C_TRI = C_IOTA + EXPERTS
C_CV = C_TRI + GROUPS * GROUPS
C_SLOT = C_CV + CAP // GROUPS
C_END = C_SLOT + 1

(PK0, PV1, RB1, PQ0, OP1A, OP1B, XT, PK1, HE, PQ1, PV0, RB0, PVA, OB, PVB, OP0A, OP0B) = range(17)
BANK = (0, 1, 0, 0, 1, 0, 1, 0, 1, 0, 1, 0, 0, 1, 0, 1, 0)
USES = 17
PROJ = (PK0, PQ0, PK1, PQ1, PVA, PVB)
LATE = (PV1, RB1, OP1A, OP1B)
TGROUPS = [(t, j, min(4, t + 1 - j)) for t in range(TILES) for j in range(0, t + 1, 4)]
NTG = len(TGROUPS)


def uses_of(n):
    if n == UNITS:
        return [PV1, RB1]
    return [k for k in range(USES) if not (n == 0 and k in LATE) and not (n == UNITS - 1 and k in PROJ)]


def before(n, k):
    if isinstance(n, int):
        return 6 + sum(len(uses_of(u)) for u in range(n)) + sum(1 for x in uses_of(n) if x < k)
    return USES * n + (before(1, 0) - USES + k)


def previous(n, k):
    old = [j for j in (uses_of(n) if isinstance(n, int) else range(k)) if j < k and BANK[j] == BANK[k]]
    if old:
        return n, old[-1]
    if isinstance(n, int) and n == 0:
        return -1, (PVA, PVB)[BANK[k]]
    return n - 1, max(j for j in range(USES) if BANK[j] == BANK[k])


class Steps:

    def __init__(self):
        self.n = 0

    def next(self, k=1):
        self.n += k
        return self.n


def layer(nc, x, wpack, epack, gate_wt, gate_bias, sh_gate, sh_up, sh_down, cols, cst, out):
    table = nc.dram_tensor("token_table", (TOK + CAP, TROW), F32, kind="Internal").ap()
    y = nc.dram_tensor("token_sum", (TOK + CAP, DM), F32, kind="Internal").ap()
    counts = nc.dram_tensor("slot_counts", (P, CAP // GROUPS), F32, kind="Internal").ap()
    x_t = x.rearrange("(q i p) d -> q p i d", p=P, i=GT)
    out_t = out.rearrange("(q i p) d -> q p i d", p=P, i=GT)
    y_t = y[0:TOK, :].rearrange("(q i p) d -> q p i d", p=P, i=GT)
    table_t = table[0:TOK, :].rearrange("(q i p) d -> q p i d", p=P, i=GT)
    table_w = table[0:TOK, :].rearrange("(t p) d -> p t d", p=P)

    with ExitStack() as ctx:
        def sb(name, shape, dt=F32, where=ctx):
            return where.enter_context(nc.sbuf_tensor(name, shape, dt))

        def sem(name):
            return ctx.enter_context(nc.semaphore(name))

        ps = ctx.enter_context(nc.psum_tensor("ps", [P, 8, CH], F32))
        score = [ps[:, 2 * i:2 * i + 2, :].rearrange("p a b -> p (a b)") for i in range(2)]
        tbank = [ps[:, 4 + i, :] for i in range(2)]
        mm = [ps[:, 6 + i, :] for i in range(2)]

        k_sb = sb("k_sb", [P, C_END])
        ident, cos_sb, sin_sb = k_sb[:, C_ID:C_ID + P], k_sb[:, C_COS:C_COS + SEQ], k_sb[:, C_SIN:C_SIN + SEQ]
        maskb = sb("maskb", [P, 2 * P], BF16)
        cols_sb = sb("cols_sb", [P, 3 * KC])
        x2h = sb("x2h", [P, KC, TOK], F32R)
        x2l = sb("x2l", [P, KC, TOK], F32R)
        acc = sb("acc", [P, KC, TOK])
        wraw = sb("wraw", [P, WROW])
        wph, wpl = sb("wph", [P, WP], F32R), sb("wpl", [P, WP], F32R)
        woh, wol = sb("woh", [P, WO], F32R), sb("wol", [P, WO], F32R)
        bqk, bvc = sb("bqk", [P, 2]), sb("bvc", [P, 1])
        ew = sb("ew", [P, EROW])
        idx = sb("idx", [CAP, EXPERTS], U32)
        qb = sb("qb", [P, 2, CH])
        qs = sb("qs", [P, 2, CH])
        ra = sb("ra", [P, 4, CH])
        rb = sb("rb", [P, CH])
        q_h = [sb("q_h0", [P, SEQ], F32R)]
        q_l = [sb("q_l0", [P, SEQ], F32R)]
        k_h = [sb("k_h0", [P, SEQ], F32R)]
        k_l = [sb("k_l0", [P, SEQ], F32R)]
        v_h = [sb("v_h0", [P, SEQ], F32R)]
        v_l = [sb("v_l0", [P, SEQ], F32R)]

        with ExitStack() as pro:
            xt = sb("xt", [P, 2, GT, DM], where=pro)
            xn = sb("xn", [P, 2, GT, DM], where=pro)
            zz = sb("zz", [P, GT, DM], where=pro)
            base = sb("base", [P, GT, DM], where=pro)
            st = sb("st", [P, GT, 6], where=pro)
            mv = sb("mv", [P, GT, 2], where=pro)
            var = sb("var", [P, GT], where=pro)
            sd = sb("sd", [P, GT], where=pro)
            rstd = sb("rstd", [P, GT], where=pro)
            nt1 = sb("nt1", [P, GT], where=pro)
            xnt = sb("xnt", [P, 2, KC, CH], where=pro)
            xnh = sb("xnh", [P, 2, KC, CH], F32R, where=pro)
            xnl = sb("xnl", [P, 2, KC, CH], F32R, where=pro)
            ztmp = sb("ztmp", [P, KC, CH], where=pro)
            sth = sb("sth", [P, CH], where=pro)
            sh = sb("sh", [P, CH], where=pro)
            shh = sb("shh", [P, 2, CH], F32R, where=pro)
            shl = sb("shl", [P, 2, CH], F32R, where=pro)
            shw = sb("shw", [P, 3, KC * FS], where=pro)
            swh = sb("swh", [P, 3, KC * FS], F32R, where=pro)
            swl = sb("swl", [P, 3, KC * FS], F32R, where=pro)
            gw = sb("gw", [P, KC, EXPERTS], where=pro)
            gb = sb("gb", [P, EXPERTS], where=pro)
            sg = sb("sg", [P, NT, EXPERTS], where=pro)
            sc = sb("sc", [P, NT, EXPERTS], where=pro)
            g8 = shw[:, 0, :].rearrange("p (a b) -> p a b", b=8)
            mt = shw[:, 1:3, :].rearrange("p a b -> p (a b)").bitcast(BF16)
            gs = sb("gs", [P, NT, GROUPS], where=pro)
            gcmp, geq = (ztmp[:, i, 0:NT * GROUPS * GROUPS].rearrange("p (t a b) -> p t a b", a=GROUPS, b=GROUPS)
                         for i in range(2))
            gsel = sb("gsel", [P, NT, GROUPS], where=pro)
            m8 = sb("m8", [P, NT, 8], where=pro)
            i8 = sb("i8", [P, NT, 8], U32, where=pro)
            i8f = sb("i8f", [P, NT, 8], where=pro)
            oneh = xnt[:, 0, :, :].rearrange("p a b -> p (a b)").bitcast(BF16).rearrange(
                "p (t k e) -> p t k e", k=TOPK, e=EXPERTS)
            m4 = xnt[:, 1, :, :].rearrange("p a b -> p (a b)").bitcast(BF16).rearrange("p (t c) -> p t c", c=P)
            mk = sb("mk", [P, NT, EXPERTS], where=pro)
            den = sb("den", [P, NT], where=pro)
            cum = xnt[:, 0, :, :].rearrange("p a b -> p (a b)").bitcast(F16)
            junk = xnt[:, 1, :, :].rearrange("p a b -> p (a b)").bitcast(F16)
            zcol = sb("zcol", [P, TROW], where=pro)
            cnt = sb("cnt", [P, CAP // GROUPS], where=pro)
            cslot = sb("cslot", [CAP, EXPERTS], where=pro)
            ceq = sb("ceq", [CAP, EXPERTS], where=pro)

        q_h.append(sb("q_h1", [P, SEQ], F32R))
        q_l.append(sb("q_l1", [P, SEQ], F32R))
        k_h.append(sb("k_h1", [P, SEQ], F32R))
        k_l.append(sb("k_l1", [P, SEQ], F32R))
        v_h.append(sb("v_h1", [P, SEQ], F32R))
        v_l.append(sb("v_l1", [P, SEQ], F32R))
        prob = sb("prob", [P, 2, SEQ])
        nmax, rsum, rinv = sb("nmax", [P, TILES]), sb("rsum", [P, TILES]), sb("rinv", [P, TILES])
        rbc = sb("rbc", [P, CH])
        ot = rbc
        oh = [sb(f"oh{c}", [P, CH], F32R) for c in range(2)]
        ol = [sb(f"ol{c}", [P, CH], F32R) for c in range(2)]
        idxc = sb("idxc", [CAP, 1], U32)
        xg = sb("xg", [CAP, TROW])
        xgt = sb("xgt", [P, KC, CAP])
        eth, eh = sb("eth", [P, CAP]), sb("eh", [P, CAP])
        ea = eth
        obs = xg[:, 0:DM]
        with ExitStack() as mid:
            pt_h = [sb(f"pt_h{c}", [P, 4 * (c + 1), CH], F32R, mid) for c in range(2)]
            pt_l = [sb(f"pt_l{c}", [P, 4 * (c + 1), CH], F32R, mid) for c in range(2)]
        fin_y = sb("fin_y", [P, NG, GT, DM])

        consts_in, w_in, ew_in, small_in = sem("consts_in"), sem("w_in"), sem("ew_in"), sem("small_in")
        x_in, rows_out, swapped = ([sem(f"{s}{i}") for i in range(2)] for s in ("x_in", "rows_out", "swapped"))
        gathered, scattered = sem("gathered"), sem("scattered")
        wts_out, base_out, trash_out = sem("wts_out"), sem("base_out"), sem("trash_out")
        cnt_out, cnt_in, yin, stored = sem("cnt_out"), sem("cnt_in"), sem("yin"), sem("stored")
        vec_step = sem("vec_step")
        var_ready, sd_ready, xn_ready, z_ready = sem("var_ready"), sem("sd_ready"), sem("xn_ready"), sem("z_ready")
        base_ready, zero_ready = sem("base_ready"), sem("zero_ready")
        pro_done, pro_free = sem("pro_done"), [sem(f"pro_free{i}") for i in range(6)]
        xnt_ready, xnh_ready, xnl_ready = sem("xnt_ready"), sem("xnh_ready"), sem("xnl_ready")
        zt_ready, x2h_ready, x2l_ready = sem("zt_ready"), sem("x2h_ready"), sem("x2l_ready")
        swh_ready, swl_ready = sem("swh_ready"), sem("swl_ready")
        tanh_ready, sh_ready, shh_ready, shl_ready = sem("tanh_ready"), sem("sh_ready"), sem("shh_ready"), sem("shl_ready")
        sg_ready, wts_ready, m4_ready, mt_ready = sem("sg_ready"), sem("wts_ready"), sem("m4_ready"), sem("mt_ready")
        cnt_ready, idx_ready, maskb_ready = sem("cnt_ready"), sem("idx_ready"), sem("maskb_ready")
        acc_ready = sem("acc_ready")
        pro_act, pro_vec, pro_pool = sem("pro_act"), sem("pro_vec"), sem("pro_pool")
        pool_passed, pe_passed = sem("pool_passed"), sem("pe_passed")
        s_done, max_done, exp_done = sem("s_done"), sem("max_done"), sem("exp_done")
        pt_done, pth_done, ptl_done = sem("pt_done"), sem("pth_done"), sem("ptl_done")
        mm_done, add_done = sem("mm_done"), sem("add_done")
        qb_done, rope_a, rope_b, rope_t, rope_h, rope_l = (sem(s) for s in
                                                          ("qb_done", "rope_a", "rope_b", "rope_t", "rope_h", "rope_l"))
        vh_done, vl_done = sem("vh_done"), sem("vl_done")
        rinv_done, rbc_done, ot_done, oh_done, ol_done = (sem(s) for s in
                                                         ("rinv_done", "rbc_done", "ot_done", "oh_done", "ol_done"))
        wph_done, wpl_done, woh_done, wol_done = (sem(s) for s in ("wph_done", "wpl_done", "woh_done", "wol_done"))
        idxc_done, xgt_done, eth_done, ea_done, eh_done, ob_done = (
            sem(s) for s in ("idxc_done", "xgt_done", "eth_done", "ea_done", "eh_done", "ob_done"))
        fin_t, fin_done = sem("fin_t"), sem("fin_done")

        pro_uses = []
        for q in range(NG):
            pro_uses += [("xt", q, 0), ("xt", q, 1), ("zt", q, 0), ("zt", q, 1), ("gate", q)]
            pro_uses += [(s, q, f) for f in range(2) for s in ("g", "u")] + [("d", q, 0), ("d", q, 1)]
        pro_uses += [("mt", q) for q in range(NG)]
        order = {u: i for i, u in enumerate(pro_uses)}

        def pbank(*u):
            return ps[:, order[u] % 6, :]

        def pcount(*u):
            return order[u] + 1

        def pfree(*u):
            return pro_free[order[u] % 6]

        block = ctx.enter_context(nc.Block())

        def for_heads(eng, body):
            body(0)
            with eng.Fori(1, HEADS - 1) as h:
                body(h)
            body(HEADS - 1)

        def swaps(sp, m):
            for p in range(4):
                sp.wait_ge(qb_done, 4 * m + p + 1)
                half = DK // 2
                sp.dma_start(qs[0:half, p % 2, :], qb[half:DK, p % 2, :]).then_inc(swapped[p % 2], 16)
                sp.dma_start(qs[half:DK, p % 2, :], qb[0:half, p % 2, :]).then_inc(swapped[p % 2], 16)

        @block.sync
        def _(sp):
            sp.dma_start(k_sb[:, :], cst).then_inc(consts_in, 16)
            sp.dma_start(cols_sb[:, :], cols).then_inc(consts_in, 16)
            for q in range(2):
                sp.dma_start(xt[:, q, :, :], x_t[q]).then_inc(x_in[q], 16)
            for q in range(NG):
                if q == 0:
                    sp.dma_start(wraw[:, :], wpack[0]).then_inc(w_in, 16)
                    sp.dma_start(gw[:, :, :], gate_wt).then_inc(small_in, 16)
                    sp.dma_start(gb[:, :], gate_bias).then_inc(small_in, 16)
                    for i, a in enumerate((sh_gate, sh_up, sh_down)):
                        sp.dma_start(shw[:, i, :], a).then_inc(small_in, 16)
                    sp.dma_start(ew[:, :], epack[0]).then_inc(ew_in, 16)
                sp.wait_ge(base_ready, q + 1)
                if q + 2 < NG:
                    sp.dma_start(xt[:, q % 2, :, :], x_t[q + 2]).then_inc(x_in[q % 2], 16)
                sp.dma_start(table_t[q, :, :, 0:DM], xn[:, q % 2, :, :]).then_inc(rows_out[q % 2], 16)
                sp.dma_start(y_t[q], base[:, :, :]).then_inc(base_out, 16)
                if q == 1:
                    swaps(sp, 0)
            sp.wait_ge(zero_ready, 1)
            sp.dma_start(table[TOK:TOK + CAP, :], zcol[0:CAP, :]).then_inc(trash_out, 16)
            sp.dma_start(y[TOK:TOK + CAP, :], zcol[0:CAP, 0:DM]).then_inc(trash_out, 16)
            sp.wait_ge(wts_ready, 1)
            sp.dma_start(table_w[:, :, DM:TROW], sg[:, :, :]).then_inc(wts_out, 16)
            sp.wait_ge(cnt_ready, CAP // GROUPS)
            sp.dma_start(counts, cnt[:, :]).then_inc(cnt_out, 16)
            sp.wait_ge(cnt_out, 16)
            J = CAP // GROUPS
            c_t = counts.rearrange("(g e) j -> g j e", g=GROUPS)
            for g in range(GROUPS):
                sp.dma_start(cslot[g * J:(g + 1) * J, :], c_t[g], allow_slow_non_contiguous=True).then_inc(cnt_in, 16)

            def body(h):
                for b in range(BATCH):
                    n = BATCH * h + b
                    last = isinstance(h, int) and n == UNITS - 1
                    if not last:
                        swaps(sp, n + 1)
                    if b == 0 and not (isinstance(h, int) and h == HEADS - 1):
                        sp.wait_ge(wol_done, h + 1)
                        sp.dma_start(wraw[:, :], wpack[h + 1]).then_inc(w_in, 16)
                    if not last:
                        sp.wait_ge(mm_done, before(n, OB) + 1)
                        sp.dma_start(ew[:, :], epack[n + 1]).then_inc(ew_in, 16)

            for_heads(sp, body)
            sp.wait_ge(scattered, 16 * UNITS)
            sp.wait_ge(mm_done, before(UNITS, 0) + 2)
            for q in range(NG):
                sp.dma_start(fin_y[:, q, :, :], y_t[q]).then_inc(yin, 16)
            for q in range(NG):
                sp.wait_ge(fin_done, KC * (q + 1))
                sp.dma_start(out_t[q], fin_y[:, q, :, :]).then_inc(stored, 16)
            sp.wait_ge(stored, 16 * NG)

        def three(eng, dst, lhs, rhs, start, stop):
            eng.matmul(dst, lhs[0], rhs[0], start=start, stop=False)
            eng.matmul(dst, lhs[0], rhs[1], start=False, stop=False)
            return eng.matmul(dst, lhs[1], rhs[0], start=False, stop=stop)

        def take(eng, n, k):
            u, j = previous(n, k)
            reader, count = {
                OP1A: (add_done, 4 * u - 1), OP1B: (add_done, 4 * u), OP0A: (add_done, 4 * u + 1),
                OP0B: (add_done, 4 * u + 2),
                PK0: (qb_done, 4 * u + 5), PQ0: (qb_done, 4 * u + 6), PK1: (qb_done, 4 * u + 7),
                PQ1: (qb_done, 4 * u + 8), PVA: (vl_done, 2 * u + 3), PVB: (vl_done, 2 * u + 4),
                XT: (xgt_done, u + 1), HE: (eh_done, u + 1), OB: (ob_done, u + 1),
                PV0: (ot_done, 2 * u + 1), PV1: (ot_done, 2 * u),
                RB0: (rbc_done, 2 * u + 1), RB1: (rbc_done, 2 * u),
            }[j]
            eng.wait_ge(reader, count)
            return mm[BANK[k]]

        def project(eng, bank, b, kind, c):
            if kind < 2:
                w0 = kind * KC * DK
                for k in range(KC):
                    w = slice(w0 + k * DK, w0 + (k + 1) * DK)
                    t = slice(b * SEQ + c * CH, b * SEQ + (c + 1) * CH)
                    last = three(eng, bank, (wph[:, w], wpl[:, w]), (x2h[:, k, t], x2l[:, k, t]), k == 0, k == KC - 1)
            else:
                w0 = 2 * KC * DK
                for i in range(GT):
                    for k in range(KC):
                        w = slice(w0 + k * DK, w0 + (k + 1) * DK)
                        t0 = b * SEQ + c * CH + i * P
                        last = three(eng, bank[:, i * P:(i + 1) * P], (x2h[:, k, t0:t0 + P], x2l[:, k, t0:t0 + P]),
                                     (wph[:, w], wpl[:, w]), k == 0, k == KC - 1)
            return last

        @block.tensor
        def _(pe):
            pe.wait_ge(consts_in, 32)

            def popen(*u):
                i = order[u]
                if i >= 6:
                    pe.wait_ge(pro_free[i % 6], i // 6)
                return pbank(*u)

            for q in range(NG):
                p = q % 2
                pe.wait_ge(xn_ready, q + 1)
                for k in range(KC):
                    bank = popen("xt", q, k)
                    for i in range(GT):
                        ins = pe.transpose(bank[:, i * P:(i + 1) * P], xn[:, p, i, k * P:(k + 1) * P], ident)
                    ins.then_inc(pro_done, 1)
                pe.wait_ge(z_ready, q + 1)
                for k in range(KC):
                    bank = popen("zt", q, k)
                    for i in range(GT):
                        ins = pe.transpose(bank[:, i * P:(i + 1) * P], zz[:, i, k * P:(k + 1) * P], ident)
                    ins.then_inc(pro_done, 1)
                pe.wait_ge(xnt_ready, KC * (q + 1))
                pe.wait_ge(small_in, 16 * 5)
                bank = popen("gate", q)
                for i in range(GT):
                    for k in range(KC):
                        ins = pe.matmul(bank[:, i * EXPERTS:(i + 1) * EXPERTS], xnt[:, p, k, i * P:(i + 1) * P],
                                        gw[:, k, :], start=(k == 0), stop=(k == KC - 1))
                ins.then_inc(pro_done, 1)
                pe.wait_ge(xnl_ready, KC * (q + 1))
                if q == 0:
                    pe.wait_ge(swl_ready, 1)
                for f in range(2):
                    for s, name in enumerate(("g", "u")):
                        bank = popen(name, q, f)
                        for k in range(KC):
                            w = slice(k * FS + f * P, k * FS + (f + 1) * P)
                            ins = three(pe, bank, (swh[:, s, w], swl[:, s, w]), (xnh[:, p, k, :], xnl[:, p, k, :]),
                                        k == 0, k == KC - 1)
                        ins.then_inc(pro_done, 1)
                if q == 1:
                    pe.wait_ge(wpl_done, 1)
                    pe.wait_ge(x2l_ready, KC * 2)
                    for i, k in enumerate(PROJ):
                        kind, c = ((1, 0), (0, 0), (1, 1), (0, 1), (2, 0), (2, 1))[i]
                        if i >= 2:
                            pe.wait_ge(qb_done, i - 1)
                        project(pe, mm[i % 2], 0, kind, c).then_inc(mm_done, 1)
                pe.wait_ge(shl_ready, 2 * (q + 1))
                for m in range(KC):
                    bank = popen("d", q, m)
                    for f in range(2):
                        w = slice(f * DM + m * P, f * DM + (m + 1) * P)
                        ins = three(pe, bank, (swh[:, 2, w], swl[:, 2, w]), (shh[:, f, :], shl[:, f, :]), f == 0, f == 1)
                    ins.then_inc(pro_done, 1)
            pe.wait_ge(m4_ready, 1)
            pe.wait_ge(maskb_ready, 1)
            for q in range(NG):
                bank = popen("mt", q)
                tb = bank.bitcast(BF16)
                for i in range(GT):
                    ins = pe.transpose(tb[:, i * P:(i + 1) * P], m4[:, q * GT + i, :], maskb[:, 0:P])
                ins.then_inc(pro_done, 1)
            pe.wait_ge(pro_act, 1)
            pe.wait_ge(pro_vec, 1)

            def scores(n, b, t):
                first = isinstance(n, int) and n == 0
                if not (first and t < 2):
                    pe.wait_ge(exp_done, TILES * n + t - 1)
                if t % 4 == 0:
                    pe.wait_ge(rope_l, 4 * n + (2, 4)[t // 4])
                dst, i = score[t % 2], slice(t * P, (t + 1) * P)
                for c in range(t // 4 + 1):
                    w = min(CH, (t + 1) * P - c * CH)
                    j = slice(c * CH, c * CH + w)
                    diag = c == t // 4
                    ins = three(pe, dst[:, j], (q_h[b][:, i], q_l[b][:, i]), (k_h[b][:, j], k_l[b][:, j]), True, not diag)
                ins = pe.matmul(dst[:, t * P:(t + 1) * P], maskb[:, 0:P], maskb[:, P:2 * P], start=False, stop=True)
                ins.then_inc(s_done, 1)

            def turn(n, t):
                pe.wait_ge(exp_done, TILES * n + t + 1)
                for g, (gt, j0, w) in enumerate(TGROUPS):
                    if gt != t:
                        continue
                    if not (isinstance(n, int) and n == 0 and g < 2):
                        pe.wait_ge(ptl_done, NTG * n + g - 1)
                    for j in range(w):
                        ins = pe.transpose(tbank[g % 2][:, j * P:(j + 1) * P],
                                           prob[:, t % 2, (j0 + j) * P:(j0 + j + 1) * P], ident)
                    ins.then_inc(pt_done, 1)

            def weighted(n, u, b, c, js):
                k = (PV0, PV1)[c]
                bank = mm[BANK[k]]
                nj = 4 * (c + 1)
                if js[0] == 0:
                    take(pe, n, k)
                    pe.wait_ge(ptl_done, NTG * u + (4, NTG)[c])
                    if c == 0:
                        pe.wait_ge(vl_done, 2 * u + 2)
                for j in js:
                    o = max(0, j - 4 * c) * P
                    v = slice(j * P, (j + 1) * P)
                    ins = three(pe, bank[:, o:CH], (v_h[b][:, v], v_l[b][:, v]), (pt_h[c][:, j, o:CH], pt_l[c][:, j, o:CH]),
                                j == 0, j == nj - 1)
                if js[-1] == nj - 1:
                    ins.then_inc(mm_done, 1)

            def spread(n, u, c):
                pe.wait_ge(rinv_done, 2 * u + c + 1)
                bank = take(pe, n, (RB0, RB1)[c])
                for i in range(4):
                    r = rinv[:, 4 * c + i:4 * c + i + 1].to_broadcast([P, P])
                    ins = pe.transpose(bank[:, i * P:(i + 1) * P], r, ident)
                ins.then_inc(mm_done, 1)

            def outproj(n, u, c):
                pe.wait_ge(ol_done, 2 * u + c + 1)
                if c == 0:
                    pe.wait_ge(wol_done, head_of(u) + 1)
                for m in range(KC):
                    bank = take(pe, n, ((OP0A, OP0B), (OP1A, OP1B))[c][m])
                    w = slice(m * P, (m + 1) * P)
                    three(pe, bank, (woh[:, w], wol[:, w]), (oh[c][:, :], ol[c][:, :]), True, True).then_inc(mm_done, 1)

            def head_of(u):
                return heads[u] if isinstance(u, int) else head[0]

            heads = {u: u // 2 for u in range(-1, UNITS)}
            head = [None]

            def next_proj(n, b, k):
                if isinstance(n, int) and n == UNITS - 1:
                    return
                kind, c = {PK0: (1, 0), PK1: (1, 1), PQ0: (0, 0), PQ1: (0, 1), PVA: (2, 0), PVB: (2, 1)}[k]
                if k == PK0 and b == 1:
                    pe.wait_ge(wpl_done, head[0] + 2)
                bank = take(pe, n, k)
                project(pe, bank, 1 - b, kind, c).then_inc(mm_done, 1)

            def expert_turn(n):
                pe.wait_ge(gathered, 16 * (n + 1))
                bank = take(pe, n, XT)
                pe.sem_inc(pe_passed, 1)
                for k in range(KC):
                    ins = pe.transpose(bank[:, k * CAP:(k + 1) * CAP], xg[:, k * P:(k + 1) * P], ident[0:CAP, 0:CAP])
                ins.then_inc(mm_done, 1)

            def expert_up(n):
                pe.wait_ge(xgt_done, n + 1)
                pe.wait_ge(ew_in, 16 * (n + 1))
                bank = take(pe, n, HE)
                for s in range(2):
                    for k in range(KC):
                        w = s * KC * FE + k * FE
                        ins = pe.matmul(bank[:, s * CAP:(s + 1) * CAP], ew[:, w:w + FE], xgt[:, k, :],
                                        start=(k == 0), stop=(k == KC - 1))
                ins.then_inc(mm_done, 1)

            def expert_down(n):
                pe.wait_ge(eh_done, n + 1)
                bank = take(pe, n, OB)
                pe.matmul(bank[0:CAP, 0:DM], eh[:, :], ew[:, 2 * KC * FE:EROW], start=True, stop=True).then_inc(mm_done, 1)

            def body(h):
                head[0] = h
                for b in range(BATCH):
                    n = BATCH * h + b
                    late = not (isinstance(n, int) and n == 0)
                    scores(n, b, 0)
                    scores(n, b, 1)
                    next_proj(n, b, PK0)
                    turn(n, 0)
                    scores(n, b, 2)
                    if late:
                        weighted(n, n - 1, 1 - b, 1, range(4))
                    turn(n, 1)
                    scores(n, b, 3)
                    if late:
                        weighted(n, n - 1, 1 - b, 1, range(4, 8))
                        spread(n, n - 1, 1)
                    turn(n, 2)
                    scores(n, b, 4)
                    next_proj(n, b, PQ0)
                    turn(n, 3)
                    scores(n, b, 5)
                    if late:
                        outproj(n, n - 1, 1)
                    expert_turn(n)
                    next_proj(n, b, PK1)
                    turn(n, 4)
                    scores(n, b, 6)
                    expert_up(n)
                    next_proj(n, b, PQ1)
                    weighted(n, n, b, 0, range(4))
                    turn(n, 5)
                    scores(n, b, 7)
                    spread(n, n, 0)
                    next_proj(n, b, PVA)
                    turn(n, 6)
                    expert_down(n)
                    next_proj(n, b, PVB)
                    outproj(n, n, 0)
                    turn(n, 7)

            for_heads(pe, body)
            u = UNITS - 1
            weighted(UNITS, u, 1, 1, range(8))
            spread(UNITS, u, 1)
            pe.wait_ge(ol_done, 2 * u + 2)
            for m in range(KC):
                w = slice(m * P, (m + 1) * P)
                dst = score[m][:, 0:CH]
                three(pe, dst, (woh[:, w], wol[:, w]), (oh[1][:, :], ol[1][:, :]), True, True).then_inc(mm_done, 1)
            pe.wait_ge(exp_done, TILES * UNITS)
            pe.wait_ge(acc_ready, 2)
            for q in range(NG):
                for i in range(GT):
                    dst = ps[:, (2 * q + i // 2) % 6, :]
                    if q == 3 and i % 2 == 0:
                        pe.wait_ge(fin_done, i // 2 + 1)
                    for m in range(KC):
                        t = (q * GT + i) * P
                        o = (i % 2) * DM + m * P
                        ins = pe.transpose(dst[:, o:o + P], acc[:, m, t:t + P], ident)
                    if i % 2:
                        ins.then_inc(fin_t, 1)

        def rope_in(act, m, b, i, bank, done):
            act.wait_ge(mm_done, done)
            if not (isinstance(m, int) and m == 0 and i < 2):
                act.wait_ge(rope_t, 4 * m + i - 1)
            s = 1 - i % 2
            act.activation(qb[:, i % 2, :], mm[bank], ACT.Identity, bias=bqk[:, s:s + 1],
                           scale=(1.0, SCALE)[i % 2]).then_inc(qb_done, 1)

        def rope_hi(act, m, b, i):
            act.wait_ge(rope_t, 4 * m + i + 1)
            dst = (k_h, q_h)[i % 2][b]
            act.activation(dst[:, (i // 2) * CH:(i // 2 + 1) * CH], ra[:, i, :], ACT.Copy).then_inc(rope_h, 1)

        def v_hi(act, m, b, c, done):
            act.wait_ge(mm_done, done)
            act.activation(v_h[b][:, c * CH:(c + 1) * CH], mm[c if isinstance(m, int) and m == 0 else BANK[(PVA, PVB)[c]]],
                           ACT.Copy).then_inc(vh_done, 1)

        @block.scalar
        def _(act):
            act.wait_ge(consts_in, 32)
            act.activation(maskb[:, :], k_sb[:, C_ID:C_MASK + P], ACT.Copy).then_inc(maskb_ready, 1)

            def drop(*u):
                act.wait_ge(pro_done, pcount(*u))
                return pbank(*u)

            for q in range(NG):
                p = q % 2
                t = slice(q * CH, (q + 1) * CH)
                for s in range(2):
                    act.wait_ge(var_ready, 2 * q + s + 1)
                    act.activation(sd[:, :], var[:, :], ACT.Sqrt).then_inc(sd_ready, 1)
                for k in range(KC):
                    bank = drop("xt", q, k)
                    if q >= 2:
                        act.wait_ge(pro_done, pcount("u", q - 2, 1))
                    act.activation(xnt[:, p, k, :], bank, ACT.Copy).then_inc(xnt_ready, 1)
                    act.wait_ge(xnt_ready, KC * q + k + 1)
                    act.activation(xnh[:, p, k, :], xnt[:, p, k, :], ACT.Copy).then_inc(pfree("xt", q, k), 1)
                for k in range(KC):
                    bank = drop("zt", q, k)
                    if q >= 1:
                        act.wait_ge(x2l_ready, KC * (q - 1) + k + 1)
                    act.activation(ztmp[:, k, :], bank, ACT.Identity, bias=cols_sb[:, KC + k:KC + k + 1],
                                   scale=cols_sb[:, k:k + 1]).then_inc(zt_ready, 1)
                    act.wait_ge(zt_ready, KC * q + k + 1)
                    act.activation(x2h[:, k, t], ztmp[:, k, :], ACT.Copy).then_inc(pfree("zt", q, k), 1)
                if q == 0:
                    act.wait_ge(small_in, 16 * 5)
                    act.activation(swh[:, :, :], shw[:, :, :], ACT.Copy).then_inc(swh_ready, 1)
                    act.wait_ge(w_in, 16)
                    act.activation(wph[:, :], wraw[:, 0:WP], ACT.Copy).then_inc(wph_done, 1)
                bank = drop("gate", q)
                act.activation(sg[:, q * GT:(q + 1) * GT, :].rearrange("p a b -> p (a b)"), bank[:, 0:GT * EXPERTS],
                               ACT.Exp, scale=-1.0).then_inc(pfree("gate", q), 1)
                for f in range(2):
                    bank = drop("g", q, f)
                    i = 2 * q + f
                    if i >= 1:
                        act.wait_ge(sh_ready, i)
                    act.activation(sth[:, :], bank, ACT.Tanh, scale=0.5).then_inc(tanh_ready, 1)
                    act.wait_ge(sh_ready, i + 1)
                    if q >= 1:
                        act.wait_ge(pro_done, pcount("d", q - 1, 1))
                    act.activation(shh[:, f, :], sh[:, :], ACT.Copy).then_inc(shh_ready, 1)
                if q == 1:
                    for i in range(4):
                        rope_in(act, 0, 0, i, i % 2, i + 1)
                    for c in range(2):
                        v_hi(act, 0, 0, c, 4 + c + 1)
                    for i in range(4):
                        rope_hi(act, 0, 0, i)
                for m in range(KC):
                    bank = drop("d", q, m)
                    act.activation(acc[:, m, t], bank, ACT.Identity,
                                   bias=cols_sb[:, 2 * KC + m:2 * KC + m + 1]).then_inc(pfree("d", q, m), 1)
            for q in range(NG):
                bank = drop("mt", q)
                act.activation(mt[:, q * CH:(q + 1) * CH], bank.bitcast(BF16)[:, 0:CH], ACT.Copy).then_inc(mt_ready, 1)
            act.wait_ge(mt_ready, NG)
            act.nop().then_inc(pro_act, 1)
            act.wait_ge(pro_vec, 1)

            def exps(n, t):
                act.wait_ge(max_done, TILES * n + t + 1)
                w = (t + 1) * P
                act.activation(prob[:, t % 2, 0:w], score[t % 2][:, 0:w], ACT.Exp, bias=nmax[:, t:t + 1],
                               accum_out=rsum[:, t:t + 1]).then_inc(exp_done, 1)

            def turned_hi(n, t):
                for g, (gt, j0, w) in enumerate(TGROUPS):
                    if gt != t:
                        continue
                    c = t // 4
                    if t % 4 == 0 and j0 == 0 and not (isinstance(n, int) and n == 0):
                        act.wait_ge(mm_done, (before(n - 1, PV0), before(n, PV1))[c] + 1)
                    act.wait_ge(pt_done, NTG * n + g + 1)
                    act.activation(pt_h[c][:, j0:j0 + w, (t % 4) * P:(t % 4 + 1) * P],
                                   tbank[g % 2][:, 0:w * P].rearrange("p (j i) -> p j i", i=P),
                                   ACT.Copy).then_inc(pth_done, 1)

            def rsum_spread(n, u, c):
                k = (RB0, RB1)[c]
                act.wait_ge(mm_done, before(n, k) + 1)
                if not (isinstance(n, int) and n == 0 and c == 0):
                    act.wait_ge(ol_done, 2 * u + c)
                act.activation(rbc[:, :], mm[BANK[k]], ACT.Copy).then_inc(rbc_done, 1)

            def out_hi(n, c):
                act.wait_ge(ot_done, 2 * n + c + 1)
                act.activation(oh[c][:, :], ot[:, :], ACT.Identity, bias=bvc[:, 0:1]).then_inc(oh_done, 1)

            def expert_tanh(n):
                act.wait_ge(mm_done, before(n, HE) + 1)
                act.activation(eth[:, :], mm[BANK[HE]][:, 0:CAP], ACT.Tanh, scale=0.5).then_inc(eth_done, 1)

            def expert_out(n):
                act.wait_ge(mm_done, before(n, OB) + 1)
                if not (isinstance(n, int) and n == 0):
                    act.wait_ge(scattered, 16 * n)
                act.activation(obs[:, :], mm[BANK[OB]][0:CAP, 0:DM], ACT.Copy,
                               scale=xg[:, bass.ds(n + DM, 1)]).then_inc(ob_done, 1)

            def body(h):
                for b in range(BATCH):
                    n = BATCH * h + b
                    more = not (isinstance(n, int) and n == UNITS - 1)

                    def piece(i):
                        if more:
                            k = PROJ[i]
                            rope_in(act, n + 1, 1 - b, i, BANK[k], before(n, k) + 1)

                    def piece_hi(i):
                        if more:
                            rope_hi(act, n + 1, 1 - b, i)

                    def value(c):
                        if more:
                            v_hi(act, n + 1, 1 - b, c, before(n, (PVA, PVB)[c]) + 1)

                    late = not (isinstance(n, int) and n == 0)
                    exps(n, 0)
                    exps(n, 1)
                    piece(0)
                    turned_hi(n, 0)
                    exps(n, 2)
                    turned_hi(n, 1)
                    exps(n, 3)
                    turned_hi(n, 2)
                    if late:
                        rsum_spread(n, n - 1, 1)
                    exps(n, 4)
                    if late:
                        out_hi(n - 1, 1)
                    piece(1)
                    turned_hi(n, 3)
                    exps(n, 5)
                    piece_hi(0)
                    piece(2)
                    if b == 0:
                        if late:
                            act.wait_ge(mm_done, before(n, OP1B) + 1)
                        act.activation(woh[:, :], wraw[:, WP:WP + WO], ACT.Copy).then_inc(woh_done, 1)
                    turned_hi(n, 4)
                    exps(n, 6)
                    expert_tanh(n)
                    piece(3)
                    piece_hi(1)
                    turned_hi(n, 5)
                    rsum_spread(n, n, 0)
                    exps(n, 7)
                    out_hi(n, 0)
                    value(0)
                    turned_hi(n, 6)
                    piece_hi(2)
                    expert_out(n)
                    value(1)
                    turned_hi(n, 7)
                    piece_hi(3)
                    if b == 0 and more and not (isinstance(h, int) and h == HEADS - 1):
                        act.wait_ge(w_in, 16 * (h + 2))
                        act.wait_ge(mm_done, before(n, PVB) + 1)
                        act.activation(wph[:, :], wraw[:, 0:WP], ACT.Copy).then_inc(wph_done, 1)

            for_heads(act, body)
            rsum_spread(UNITS, UNITS - 1, 1)
            out_hi(UNITS - 1, 1)

        def rope_lo(dve, m, b, i):
            dve.wait_ge(rope_h, 4 * m + i + 1)
            s = slice((i // 2) * CH, (i // 2 + 1) * CH)
            hi, lo = ((k_h, k_l), (q_h, q_l))[i % 2]
            dve.tensor_tensor(lo[b][:, s], ra[:, i, :], hi[b][:, s].bitcast(F32), ALU.subtract).then_inc(rope_l, 1)

        def v_lo(dve, m, b, c):
            k = c if isinstance(m, int) and m == 0 else BANK[(PVA, PVB)[c]]
            dve.wait_ge(vh_done, 2 * m + c + 1)
            dve.tensor_tensor(v_l[b][:, c * CH:(c + 1) * CH], mm[k], v_h[b][:, c * CH:(c + 1) * CH].bitcast(F32),
                              ALU.subtract).then_inc(vl_done, 1)

        def w_lo(dve, h):
            dve.wait_ge(wph_done, h + 1)
            dve.tensor_scalar(bqk[:, 0:1], wraw[:, WP + WO:WP + WO + 1], SCALE, None, ALU.mult)
            dve.tensor_copy(bqk[:, 1:2], wraw[:, WP + WO + 1:WP + WO + 2])
            dve.tensor_tensor(wpl[:, :], wraw[:, 0:WP], wph[:, :].bitcast(F32), ALU.subtract).then_inc(wpl_done, 1)

        @block.vector
        def _(dve):
            step = Steps()

            def layernorm(q, s, src, dst, ready):
                for i in range(GT):
                    ins = dve.bn_stats(st[:, i, :], src[:, i, :])
                ins.then_inc(vec_step, 1)
                dve.wait_ge(vec_step, step.next())
                for i in range(GT):
                    ins = dve.bn_aggr(mv[:, i, :], st[:, i, :])
                ins.then_inc(vec_step, 1)
                dve.wait_ge(vec_step, step.next())
                dve.tensor_scalar(var[:, :], mv[:, :, 1], EPS, None, ALU.add).then_inc(var_ready, 1)
                dve.wait_ge(sd_ready, 2 * q + s + 1)
                dve.reciprocal(rstd[:, :], sd[:, :]).then_inc(vec_step, 1)
                dve.wait_ge(vec_step, step.next())
                dve.tensor_tensor(nt1[:, :], rstd[:, :], rstd[:, :], ALU.mult).then_inc(vec_step, 1)
                dve.wait_ge(vec_step, step.next())
                dve.scalar_tensor_tensor(out=nt1[:, :], in0=nt1[:, :], scalar=-0.5, in1=var[:, :],
                                         op0=ALU.mult, op1=ALU.mult).then_inc(vec_step, 1)
                dve.wait_ge(vec_step, step.next())
                dve.scalar_tensor_tensor(out=rstd[:, :], in0=nt1[:, :], scalar=1.5, in1=rstd[:, :],
                                         op0=ALU.add, op1=ALU.mult).then_inc(vec_step, 1)
                dve.wait_ge(vec_step, step.next())
                for i in range(GT):
                    ins = dve.tensor_scalar(dst[:, i, :], src[:, i, :], mv[:, i, 0:1], rstd[:, i:i + 1],
                                            ALU.subtract, ALU.mult)
                ins.then_inc(ready, 1)

            dve.memset(zcol[:, :], 0.0).then_inc(zero_ready, 1)
            for q in range(NG):
                p = q % 2
                dve.wait_ge(x_in[p], 16 * (q // 2 + 1))
                if q >= 2:
                    dve.wait_ge(rows_out[p], 16)
                    dve.wait_ge(pro_done, pcount("xt", q - 2, 1))
                layernorm(q, 0, xt[:, p], xn[:, p], xn_ready)
                dve.wait_ge(xn_ready, q + 1)
                if q >= 1:
                    dve.wait_ge(pro_done, pcount("zt", q - 1, 1))
                layernorm(q, 1, xn[:, p], zz, z_ready)
                if q == 0:
                    dve.wait_ge(swh_ready, 1)
                    dve.tensor_tensor(swl[:, :, :], shw[:, :, :], swh[:, :, :].bitcast(F32), ALU.subtract).then_inc(swl_ready, 1)
                    w_lo(dve, 0)
                for k in range(KC):
                    dve.wait_ge(pro_free[order["xt", q, k] % 6], order["xt", q, k] // 6 + 1)
                    if q >= 2:
                        dve.wait_ge(pro_done, pcount("u", q - 2, 1))
                    dve.tensor_tensor(xnl[:, p, k, :], xnt[:, p, k, :], xnh[:, p, k, :].bitcast(F32),
                                      ALU.subtract).then_inc(xnl_ready, 1)
                t = slice(q * CH, (q + 1) * CH)
                for k in range(KC):
                    dve.wait_ge(pro_free[order["zt", q, k] % 6], order["zt", q, k] // 6 + 1)
                    dve.tensor_tensor(x2l[:, k, t], ztmp[:, k, :], x2h[:, k, t].bitcast(F32), ALU.subtract).then_inc(x2l_ready, 1)
                for f in range(2):
                    i = 2 * q + f
                    dve.wait_ge(tanh_ready, i + 1)
                    dve.scalar_tensor_tensor(out=sth[:, :], in0=sth[:, :], scalar=1.0, in1=pbank("g", q, f),
                                             op0=ALU.add, op1=ALU.mult).then_inc(pfree("g", q, f), 1)
                    dve.wait_ge(pfree("g", q, f), order["g", q, f] // 6 + 1)
                    dve.wait_ge(pro_done, pcount("u", q, f))
                    if i >= 1:
                        dve.wait_ge(shh_ready, i)
                        dve.wait_ge(shl_ready, i)
                    dve.scalar_tensor_tensor(out=sh[:, :], in0=sth[:, :], scalar=0.5, in1=pbank("u", q, f),
                                             op0=ALU.mult, op1=ALU.mult).then_inc(pfree("u", q, f), 1)
                    dve.wait_ge(pfree("u", q, f), order["u", q, f] // 6 + 1)
                    dve.engine_nop().then_inc(sh_ready, 1)
                    dve.wait_ge(sh_ready, i + 1)
                    dve.wait_ge(shh_ready, i + 1)
                    dve.tensor_tensor(shl[:, f, :], sh[:, :], shh[:, f, :].bitcast(F32), ALU.subtract).then_inc(shl_ready, 1)
                if q == 1:
                    for c in range(2):
                        v_lo(dve, 0, 0, c)
                    for i in range(4):
                        rope_lo(dve, 0, 0, i)
            dve.wait_ge(pfree("gate", 3), order["gate", 3] // 6 + 1)
            for q in range(3):
                dve.wait_ge(pfree("gate", q), order["gate", q] // 6 + 1)
            dve.tensor_scalar(sg[:, :, :], sg[:, :, :], 1.0, None, ALU.add).then_inc(vec_step, 1)
            dve.wait_ge(vec_step, step.next())
            dve.reciprocal(sg[:, :, :], sg[:, :, :]).then_inc(vec_step, 1)
            dve.wait_ge(vec_step, step.next())
            dve.tensor_tensor(sc[:, :, :], sg[:, :, :], gb[:, :].unsqueeze(1).to_broadcast([P, NT, EXPERTS]),
                              ALU.add).then_inc(vec_step, 1)
            dve.wait_ge(vec_step, step.next())
            scg = sc[:, :, :].rearrange("p t (g e) -> p (t g) e", g=GROUPS)
            for i in range(NT * GROUPS):
                ins = dve.max(g8[:, i, :], scg[:, i, :])
            ins.then_inc(vec_step, 1)
            dve.wait_ge(vec_step, step.next())
            gsf = gs[:, :, :].rearrange("p t g -> p (t g)")
            dve.tensor_tensor(gsf, g8[:, :, 0], g8[:, :, 1], ALU.add).then_inc(vec_step, 1)
            dve.wait_ge(vec_step, step.next())
            other = gs[:, :, :].unsqueeze(2).to_broadcast([P, NT, GROUPS, GROUPS])
            own = gs[:, :, :].unsqueeze(3).to_broadcast([P, NT, GROUPS, GROUPS])
            tri = k_sb[:, C_TRI:C_TRI + GROUPS * GROUPS].rearrange("p (a b) -> p a b", a=GROUPS)
            dve.tensor_tensor(gcmp[:, :, :, :], other, own, ALU.is_gt)
            dve.tensor_tensor(geq[:, :, :, :], other, own, ALU.is_equal).then_inc(vec_step, 1)
            dve.wait_ge(vec_step, step.next())
            dve.tensor_tensor(geq[:, :, :, :], geq[:, :, :, :], tri.unsqueeze(1).to_broadcast([P, NT, GROUPS, GROUPS]),
                              ALU.mult).then_inc(vec_step, 1)
            dve.wait_ge(vec_step, step.next())
            dve.tensor_tensor(gcmp[:, :, :, :], gcmp[:, :, :, :], geq[:, :, :, :], ALU.add).then_inc(vec_step, 1)
            dve.wait_ge(vec_step, step.next())
            dve.tensor_reduce(gsel[:, :, :], gcmp[:, :, :, :], AX.X, ALU.add).then_inc(vec_step, 1)
            dve.wait_ge(vec_step, step.next())
            dve.tensor_scalar(gsel[:, :, :], gsel[:, :, :], float(TOPG), None, ALU.is_lt).then_inc(vec_step, 1)
            dve.wait_ge(vec_step, step.next())
            self_g = gsel[:, :, :].rearrange("p t g -> p (t g)").unsqueeze(2).to_broadcast([P, NT * GROUPS, EG])
            dve.tensor_tensor(scg, scg, self_g, ALU.mult).then_inc(vec_step, 1)
            dve.wait_ge(vec_step, step.next())
            for t in range(NT):
                ins = dve.max(m8[:, t, :], sc[:, t, :])
            ins.then_inc(vec_step, 1)
            dve.wait_ge(vec_step, step.next())
            for t in range(NT):
                ins = dve.max_index(i8[:, t, :], m8[:, t, :], sc[:, t, :])
            ins.then_inc(vec_step, 1)
            dve.wait_ge(vec_step, step.next())
            dve.tensor_copy(i8f[:, :, :], i8[:, :, :]).then_inc(vec_step, 1)
            dve.wait_ge(vec_step, step.next())
            io = k_sb[:, C_IOTA:C_IOTA + EXPERTS]
            for k in range(TOPK):
                ins = dve.tensor_tensor(oneh[:, :, k, :], io.unsqueeze(1).to_broadcast([P, NT, EXPERTS]),
                                        i8f[:, :, k:k + 1].to_broadcast([P, NT, EXPERTS]), ALU.is_equal)
            ins.then_inc(vec_step, 1)
            dve.wait_ge(vec_step, step.next())
            dve.tensor_reduce(mk[:, :, :], oneh[:, :, :, :].rearrange("p t k e -> p t e k"), AX.X, ALU.add).then_inc(vec_step, 1)
            dve.wait_ge(vec_step, step.next())
            for g in range(GROUPS):
                ins = dve.tensor_copy(m4[:, :, g * EXPERTS:(g + 1) * EXPERTS], mk[:, :, :])
            ins.then_inc(m4_ready, 1)
            dve.tensor_tensor(sg[:, :, :], sg[:, :, :], mk[:, :, :], ALU.mult).then_inc(vec_step, 1)
            dve.wait_ge(vec_step, step.next())
            dve.tensor_reduce(den[:, :], sg[:, :, :], AX.X, ALU.add).then_inc(vec_step, 1)
            dve.wait_ge(vec_step, step.next())
            dve.tensor_scalar(den[:, :], den[:, :], 1e-20, None, ALU.add).then_inc(vec_step, 1)
            dve.wait_ge(vec_step, step.next())
            dve.reciprocal(den[:, :], den[:, :]).then_inc(vec_step, 1)
            dve.wait_ge(vec_step, step.next())
            dve.scalar_tensor_tensor(out=sg[:, :, :], in0=sg[:, :, :], scalar=ROUTE_SCALE,
                                     in1=den[:, :].unsqueeze(2).to_broadcast([P, NT, EXPERTS]),
                                     op0=ALU.mult, op1=ALU.mult).then_inc(wts_ready, 1)
            dve.wait_ge(mt_ready, NG)
            dve.tensor_tensor_scan(cum, mt[:, :], zcol[:, 0:1].to_broadcast([P, TOK]), 0.0,
                                   ALU.add, ALU.add).then_inc(vec_step, 1)
            dve.wait_ge(vec_step, step.next())
            for j in range(CAP // GROUPS):
                if j >= 1:
                    dve.wait_ge(cnt_ready, j)
                dve.tensor_scalar(junk, cum, k_sb[:, C_CV + j:C_CV + j + 1], 0.0, ALU.is_le, ALU.add,
                                  accum_out=cnt[:, j:j + 1]).then_inc(cnt_ready, 1)
            dve.wait_ge(cnt_in, 16 * GROUPS)
            dve.tensor_scalar(ceq[:, :], cslot[:, :], float(TOK), k_sb[0:CAP, C_SLOT:C_SLOT + 1],
                              ALU.is_equal, ALU.mult).then_inc(vec_step, 1)
            dve.wait_ge(vec_step, step.next())
            dve.tensor_tensor(idx[:, :], cslot[:, :], ceq[:, :], ALU.add).then_inc(idx_ready, 1)
            dve.wait_ge(idx_ready, 1)
            for p in range(2):
                dve.wait_ge(rows_out[p], 32)
            dve.wait_ge(base_out, 16 * NG)
            dve.wait_ge(trash_out, 32)
            dve.wait_ge(wts_out, 16)
            dve.wait_ge(cnt_ready, CAP // GROUPS)
            dve.wait_ge(pro_done, len(pro_uses))
            dve.wait_ge(pro_pool, 1)
            dve.wait_ge(pro_act, 1)
            dve.engine_nop().then_inc(pro_vec, 1)

            def maxes(n, t):
                dve.wait_ge(s_done, TILES * n + t + 1)
                dve.tensor_reduce(nmax[:, t:t + 1], score[t % 2][:, 0:(t + 1) * P], AX.X, ALU.max,
                                  negate=True).then_inc(max_done, 1)

            def turned_lo(n, t):
                for g, (gt, j0, w) in enumerate(TGROUPS):
                    if gt != t:
                        continue
                    c = t // 4
                    i = slice((t % 4) * P, (t % 4 + 1) * P)
                    dve.wait_ge(pth_done, NTG * n + g + 1)
                    dve.tensor_tensor(pt_l[c][:, j0:j0 + w, i], tbank[g % 2][:, 0:w * P].rearrange("p (j i) -> p j i", i=P),
                                      pt_h[c][:, j0:j0 + w, i].bitcast(F32), ALU.subtract).then_inc(ptl_done, 1)

            def add_out(n, u_b, c):
                for m in range(KC):
                    k = ((OP0A, OP0B), (OP1A, OP1B))[c][m]
                    dve.wait_ge(mm_done, before(n, k) + 1)
                    t = slice(u_b * SEQ + c * CH, u_b * SEQ + (c + 1) * CH)
                    dve.tensor_tensor(acc[:, m, t], mm[BANK[k]], acc[:, m, t], ALU.add).then_inc(add_done, 1)

            def recips(n, c):
                dve.wait_ge(exp_done, TILES * n + 4 * c + 4)
                dve.reciprocal(rinv[:, 4 * c:4 * c + 4], rsum[:, 4 * c:4 * c + 4]).then_inc(rinv_done, 1)

            def out_scaled(n, c):
                k = (PV0, PV1)[c]
                dve.wait_ge(rbc_done, 2 * n + c + 1)
                dve.tensor_tensor(ot[:, :], mm[BANK[k]], rbc[:, :], ALU.mult).then_inc(ot_done, 1)

            def out_lo(n, c):
                dve.wait_ge(oh_done, 2 * n + c + 1)
                dve.scalar_tensor_tensor(out=ol[c][:, :], in0=ot[:, :], scalar=bvc[:, 0:1], in1=oh[c][:, :].bitcast(F32),
                                         op0=ALU.add, op1=ALU.subtract).then_inc(ol_done, 1)

            def expert_copy(n):
                dve.wait_ge(mm_done, before(n, XT) + 1)
                dve.tensor_copy(xgt[:, :, :].rearrange("p a b -> p (a b)"), mm[BANK[XT]][:, 0:KC * CAP]).then_inc(xgt_done, 1)

            def expert_gate(n):
                dve.wait_ge(eth_done, n + 1)
                bank = mm[BANK[HE]]
                dve.scalar_tensor_tensor(out=ea[:, :], in0=eth[:, :], scalar=1.0, in1=bank[:, 0:CAP],
                                         op0=ALU.add, op1=ALU.mult).then_inc(ea_done, 1)
                dve.wait_ge(ea_done, n + 1)
                dve.scalar_tensor_tensor(out=eh[:, :], in0=ea[:, :], scalar=0.5, in1=bank[:, CAP:2 * CAP],
                                         op0=ALU.mult, op1=ALU.mult).then_inc(eh_done, 1)

            def body(h):
                for b in range(BATCH):
                    n = BATCH * h + b
                    more = not (isinstance(n, int) and n == UNITS - 1)
                    late = not (isinstance(n, int) and n == 0)
                    maxes(n, 0)
                    maxes(n, 1)
                    turned_lo(n, 0)
                    maxes(n, 2)
                    turned_lo(n, 1)
                    maxes(n, 3)
                    turned_lo(n, 2)
                    maxes(n, 4)
                    if late:
                        out_scaled(n - 1, 1)
                        out_lo(n - 1, 1)
                    turned_lo(n, 3)
                    maxes(n, 5)
                    recips(n, 0)
                    if late:
                        add_out(n, 1 - b, 1)
                    if more:
                        rope_lo(dve, n + 1, 1 - b, 0)
                    expert_copy(n)
                    if b == 0:
                        dve.wait_ge(woh_done, h + 1)
                        dve.tensor_copy(bvc[:, :], wraw[:, WP + WO + 2:WROW])
                        dve.tensor_tensor(wol[:, :], wraw[:, WP:WP + WO], woh[:, :].bitcast(F32),
                                          ALU.subtract).then_inc(wol_done, 1)
                    turned_lo(n, 4)
                    maxes(n, 6)
                    expert_gate(n)
                    if more:
                        rope_lo(dve, n + 1, 1 - b, 1)
                    turned_lo(n, 5)
                    out_scaled(n, 0)
                    maxes(n, 7)
                    out_lo(n, 0)
                    if more:
                        v_lo(dve, n + 1, 1 - b, 0)
                    turned_lo(n, 6)
                    if more:
                        rope_lo(dve, n + 1, 1 - b, 2)
                        v_lo(dve, n + 1, 1 - b, 1)
                    recips(n, 1)
                    add_out(n, b, 0)
                    turned_lo(n, 7)
                    if more:
                        rope_lo(dve, n + 1, 1 - b, 3)
                    if b == 0 and not (isinstance(h, int) and h == HEADS - 1):
                        w_lo(dve, h + 1)

            for_heads(dve, body)
            out_scaled(UNITS - 1, 1)
            out_lo(UNITS - 1, 1)
            for m in range(KC):
                t = slice(TOK - CH, TOK)
                dve.wait_ge(mm_done, before(UNITS, 0) + 2 + m + 1)
                dve.tensor_tensor(acc[:, m, t], score[m][:, 0:CH], acc[:, m, t], ALU.add).then_inc(acc_ready, 1)
            for q in range(NG):
                dve.wait_ge(yin, 16 * NG)
                for i in range(2):
                    dve.wait_ge(fin_t, 2 * q + i + 1)
                    dst = fin_y[:, q, 2 * i:2 * i + 2, :].rearrange("p a b -> p (a b)")
                    dve.tensor_tensor(dst, ps[:, (2 * q + i) % 6, :], dst, ALU.add).then_inc(fin_done, 1)

        def rope(pool, m, i):
            c = slice((i // 2) * CH, (i // 2 + 1) * CH)
            pool.wait_ge(qb_done, 4 * m + i + 1)
            if not (isinstance(m, int) and m == 0):
                pool.wait_ge(rope_l, 4 * m + i - 3)
            pool.tensor_tensor(ra[:, i, :], qb[:, i % 2, :], cos_sb[:, c], ALU.mult).then_inc(rope_a, 1)
            pool.wait_ge(swapped[i % 2], 32 * (2 * m + i // 2 + 1))
            if not (isinstance(m, int) and m == 0 and i == 0):
                pool.wait_ge(rope_t, 4 * m + i)
            pool.tensor_tensor(rb[:, :], qs[:, i % 2, :], sin_sb[:, c], ALU.mult).then_inc(rope_b, 1)
            pool.wait_ge(rope_a, 4 * m + i + 1)
            pool.wait_ge(rope_b, 4 * m + i + 1)
            pool.tensor_tensor(ra[:, i, :], ra[:, i, :], rb[:, :], ALU.add).then_inc(rope_t, 1)

        @block.gpsimd
        def _(pool):
            for q in range(NG):
                pool.wait_ge(xn_ready, q + 1)
                if q >= 1:
                    pool.wait_ge(base_out, 16 * q)
                pool.tensor_tensor(base[:, :, :], xt[:, q % 2, :, :], xn[:, q % 2, :, :], ALU.add).then_inc(base_ready, 1)
                if q == 1:
                    pool.wait_ge(consts_in, 32)
                    for i in range(4):
                        rope(pool, 0, i)
            pool.wait_ge(base_ready, NG)
            pool.wait_ge(rope_t, 4)
            pool.engine_nop().then_inc(pro_pool, 1)
            pool.wait_ge(pro_vec, 1)

            def body(h):
                for b in range(BATCH):
                    n = BATCH * h + b
                    if not (isinstance(n, int) and n == 0):
                        pool.wait_ge(scattered, 16 * n)
                    pool.tensor_copy(idxc[:, :], idx[:, bass.ds(n, 1)]).then_inc(idxc_done, 1)
                    pool.wait_ge(idxc_done, n + 1)
                    pool.sem_inc(pool_passed, 1)
                    pool.indirect_dma_start(xg[:, :], None, table[:, :],
                                            bass.IndirectOffsetOnAxis(ap=idxc[:, 0:1], axis=0)).then_inc(gathered, 16)
                    if not (isinstance(n, int) and n == UNITS - 1):
                        for i in range(4):
                            rope(pool, n + 1, i)
                    pool.wait_ge(ob_done, n + 1)
                    pool.sem_inc(pool_passed, 1)
                    pool.indirect_dma_start(y[:, :], bass.IndirectOffsetOnAxis(ap=idxc[:, 0:1], axis=0), obs[:, :],
                                            None, compute_op=ALU.add).then_inc(scattered, 16)

            for_heads(pool, body)

    return


def kernel(**inputs):
    import numpy as np
    import concourse.bacc as bacc
    from concourse.bass_utils import run_bass_kernel_spmd

    a = {k.replace("L0_attn_", "").replace("L0_ffn_", "f_"): np.asarray(v) for k, v in inputs.items()}

    def turned(w):
        return w.reshape(HEADS, DK, KC, P).transpose(0, 3, 2, 1).reshape(HEADS, P, KC * DK)

    def chunked(w):
        return w.reshape(-1, P, w.shape[-1]).transpose(1, 0, 2).reshape(P, -1)

    def column(v):
        return v.reshape(-1, P).T

    wpack = np.concatenate(
        [turned(a["wq"]), turned(a["wk"]), turned(a["wv"]), a["wo"].reshape(DM, HEADS, DK).transpose(1, 2, 0)]
        + [a[b].reshape(HEADS, DK, 1) for b in ("bq", "bk", "bv")], axis=2)
    epack = np.concatenate([w.reshape(EXPERTS, -1, P, w.shape[-1]).transpose(0, 2, 1, 3).reshape(EXPERTS, P, -1)
                            for w in (a["f_w1"], a["f_w3"], a["f_w2"])], axis=2)
    gate_wt = a["f_gate_w"].T.reshape(KC, P, EXPERTS).transpose(1, 0, 2)
    gate_bias = np.broadcast_to(a["f_gate_bias"], (P, EXPERTS))
    cols = np.concatenate([column(a["ln_g"]), column(a["ln_b"]), column(a["bo"])], axis=1)

    f4 = np.float32
    theta = f4(1.0) / f4(10000.0) ** (np.arange(0, DK, 2, dtype=f4) / f4(DK))
    freq = (np.arange(SEQ, dtype=f4)[:, None] * theta[None, :]).astype(f4)
    cos, sin = np.cos(freq).T, np.sin(freq).T
    cst = np.zeros((P, C_END), f4)
    cst[:, C_ID:C_ID + P] = np.eye(P)
    cst[:, C_MASK:C_MASK + P] = NEG * np.triu(np.ones((P, P)), 1)
    cst[:, C_COS:C_COS + SEQ] = np.concatenate([cos, cos])
    cst[:, C_SIN:C_SIN + SEQ] = np.concatenate([-sin, sin])
    cst[:, C_IOTA:C_IOTA + EXPERTS] = np.arange(EXPERTS)
    cst[:, C_TRI:C_TRI + GROUPS * GROUPS] = np.tril(np.ones((GROUPS, GROUPS)), -1).reshape(-1)
    J = CAP // GROUPS
    cst[:, C_CV:C_CV + J] = (np.arange(P) // EXPERTS * J)[:, None] + np.arange(J)
    cst[:, C_SLOT] = np.arange(P)

    nc = bacc.Bacc("TRN2", target_bir_lowering=False, num_devices=1)
    arrays, args = {}, []
    for name, v in (("x", a["h"].reshape(TOK, DM)), ("wpack", wpack), ("epack", epack), ("gate_wt", gate_wt),
                    ("gate_bias", gate_bias), ("sh_gate", chunked(a["f_shared_gate"])),
                    ("sh_up", chunked(a["f_shared_up"])), ("sh_down", chunked(a["f_shared_down"])),
                    ("cols", cols), ("cst", cst)):
        v = np.ascontiguousarray(v)
        arrays[name] = v
        args.append(nc.dram_tensor(name, v.shape, mybir.dt.from_np(v.dtype), kind="ExternalInput").ap())
    out = nc.dram_tensor("out", (TOK, DM), F32, kind="ExternalOutput").ap()
    layer(nc, *args, out)
    r = run_bass_kernel_spmd(nc, [arrays], core_ids=[0])
    return r.results[0]["out"].reshape(BATCH, SEQ, DM)
```
